# Optimizing a Trainium2 kernel written in Bass

```python
import numpy as np
import jax
import jax.numpy as jnp

def _softmax(x, axis=-1):
    return jax.nn.softmax(x, axis=axis)

def _gelu(x):
    return jax.nn.gelu(x, approximate=True)

def _silu(x):
    return jax.nn.silu(x)

def _sigmoid(x):
    return jax.nn.sigmoid(x)

def _layernorm(x, axis=-1, eps=1e-05):
    m = jnp.mean(x, axis=axis, keepdims=True)
    v = jnp.var(x, axis=axis, keepdims=True)
    return (x - m) / jnp.sqrt(v + eps)

def _scatter_add(tgt, idx, src, axis=0):
    return tgt.at[idx].add(src)

def _segment_sum(src, seg, n):
    return jax.ops.segment_sum(src, seg, n)
kernel_name = 'mk_rec_standalone_d1_rec_r8_199663'

def setup_inputs(seed: int=0):
    np.random.seed(seed)
    _w = jnp.asarray

    def _rec_inputs():
        import jax
        import jax.numpy as jnp
        _rk = jax.random.key(seed)
        r_input_data = jax.random.uniform(jax.random.fold_in(_rk, 1), (1024, 12500), jnp.float32, 0.0, 1)
        return r_input_data
    r_input_data = _rec_inputs()

    def _L0_rec_setup():
        import jax, jax.numpy as jnp
        import numpy as np
        B, N_DIMS, EMBED_DIM = (1024, 12500, 16)
        H1, H2 = (128, 64)

        def _xavier(key, shape):
            fan_in, fan_out = (shape[-1], shape[-2] if len(shape) > 1 else shape[-1])
            lim = jnp.sqrt(6.0 / (fan_in + fan_out)).astype(jnp.float32)
            return jax.random.uniform(key, shape, jnp.float32, -lim, lim)
        key = jax.random.key(seed)
        ks = jax.random.split(key, 9)
        input_data = jax.random.uniform(ks[0], (B, N_DIMS), jnp.float32)
        W_lin = _xavier(ks[1], (1, N_DIMS))
        b_lin = jnp.zeros((1,), jnp.float32)
        factors = _xavier(ks[2], (N_DIMS, EMBED_DIM))
        W1 = _xavier(ks[3], (H1, EMBED_DIM))
        b1 = jnp.zeros((H1,), jnp.float32)
        W2 = _xavier(ks[4], (H2, H1))
        b2 = jnp.zeros((H2,), jnp.float32)
        W3 = _xavier(ks[5], (1, H2))
        b3 = jnp.zeros((1,), jnp.float32)
        return {'input_data': input_data, 'W_lin': W_lin, 'b_lin': b_lin, 'factors': factors, 'W1': W1, 'b1': b1, 'W2': W2, 'b2': b2, 'W3': W3, 'b3': b3}
    _L0_rec_all = _L0_rec_setup()
    _L0_rec_in = {k: v for k, v in _L0_rec_all.items() if k in ('W_lin', 'b_lin', 'factors', 'W1', 'b1', 'W2', 'b2', 'W3', 'b3')}
    del _L0_rec_all
    return {'r_input_data': r_input_data, 'L0_rec_W_lin': _L0_rec_in['W_lin'], 'L0_rec_b_lin': _L0_rec_in['b_lin'], 'L0_rec_factors': _L0_rec_in['factors'], 'L0_rec_W1': _L0_rec_in['W1'], 'L0_rec_b1': _L0_rec_in['b1'], 'L0_rec_W2': _L0_rec_in['W2'], 'L0_rec_b2': _L0_rec_in['b2'], 'L0_rec_W3': _L0_rec_in['W3'], 'L0_rec_b3': _L0_rec_in['b3']}

def reference(r_input_data, L0_rec_W_lin, L0_rec_b_lin, L0_rec_factors, L0_rec_W1, L0_rec_b1, L0_rec_W2, L0_rec_b2, L0_rec_W3, L0_rec_b3):
    import jax
    import jax.numpy as jnp

    def _L0_rec_ref(input_data, W_lin, b_lin, factors, W1, b1, W2, b2, W3, b3):
        import jax, jax.numpy as jnp
        import numpy as np
        B, N_DIMS, EMBED_DIM = (1024, 12500, 16)
        H1, H2 = (128, 64)

        def _xavier(key, shape):
            fan_in, fan_out = (shape[-1], shape[-2] if len(shape) > 1 else shape[-1])
            lim = jnp.sqrt(6.0 / (fan_in + fan_out)).astype(jnp.float32)
            return jax.random.uniform(key, shape, jnp.float32, -lim, lim)
        x_reg = input_data @ W_lin.T + b_lin
        emb = input_data @ factors
        sum_squared = jnp.square(emb.sum(axis=1))
        squared_sum = (jnp.square(input_data) @ jnp.square(factors)).sum(axis=1)
        h = jax.nn.relu(emb @ W1.T + b1)
        h = jax.nn.relu(h @ W2.T + b2)
        dnn_out = h @ W3.T + b3
        x = x_reg + 0.5 * (sum_squared - squared_sum)[:, None] + dnn_out
        x = 0.5 + jax.nn.sigmoid(x) * 5.0
        return x.squeeze()
    y = _L0_rec_ref(r_input_data, L0_rec_W_lin, L0_rec_b_lin, L0_rec_factors, L0_rec_W1, L0_rec_b1, L0_rec_W2, L0_rec_b2, L0_rec_W3, L0_rec_b3)
    return y

_drawn_inputs = setup_inputs


def setup_inputs(seed=0):
    import zlib

    import numpy as np

    out = dict(_drawn_inputs(seed))
    spreads = {'L0_rec_b1': (0.0, 2.0), 'L0_rec_b2': (0.0, 2.0)}
    factors = {'L0_rec_W2': 4.11,
     'r_input_data': 2.809,
     'L0_rec_W_lin': 8.0,
     'L0_rec_factors': 3.77,
     'L0_rec_W1': 4.883}
    for name, (base, spread) in spreads.items():
        noise = np.random.default_rng([zlib.crc32(name.encode()), seed]).standard_normal(out[name].shape)
        drawn = base * np.exp(spread * noise) if base else spread * noise
        out[name] = jnp.asarray(drawn.astype(out[name].dtype))
    for name, factor in factors.items():
        out[name] = (out[name] * factor).astype(out[name].dtype)
    return out
```

```python
from contextlib import ExitStack

import concourse.bass as bass
from concourse import mybir

ALU = mybir.AluOpType
ACT = mybir.ActivationFunctionType
AX = mybir.AxisListType
F32 = mybir.dt.float32
BF16 = mybir.dt.bfloat16

B, N, EMB = 1024, 12500, 16
H1, H2 = 128, 64
P = 128

CHUNKS = 2
RING = 8
GROUPS = (N - P) // (P * CHUNKS)
ROUNDS = GROUPS // RING
LAST = N - P - GROUPS * P * CHUNKS
assert ROUNDS * RING == GROUPS and 0 < LAST <= P and RING % 4 == 0

LIN = EMB + 1
WC = LIN + 1

HALF = B // 2
QUART = HALF // 2
SQ = 2
DVE_PER_PAIR = 2 * CHUNKS - 1

C_W1 = 0
C_W2 = C_W1 + 2 * H1
C_B1 = C_W2 + H2
C_B2 = C_B1 + 1
C_W3 = C_B2 + 1
C_BLIN = C_W3 + 2
C_B3 = C_BLIN + 1
C_SX = C_B3 + 1
C_SE = C_SX + 2
C_SS = C_SE + 2
C_NH = C_SS + 2
C_ALL = C_NH + 1


def fm_kernel(nc, xT, w_all, w_last, params, out):
    x_first = xT[0:P, :]
    x_groups = xT[P:P + GROUPS * P * CHUNKS, :].rearrange("(g p c) b -> g p (c b)", p=P, c=CHUNKS)
    x_last = xT[N - LAST:N, :]
    out_rows = out.rearrange("(q b) -> q b", b=QUART)

    with ExitStack() as ctx:
        def sb(name, shape, dt=F32):
            return ctx.enter_context(nc.sbuf_tensor(name, shape, dt))

        def bank(name):
            return ctx.enter_context(nc.psum_tensor(name, [P, HALF], F32))

        def sem(name):
            return ctx.enter_context(nc.semaphore(name))

        xf = sb("xf", [P, B])
        xr = sb("xr", [P, RING, CHUNKS, B])
        xl = sb("xl", [P, B])
        w = sb("w", [P, 1 + GROUPS * CHUNKS, WC])
        wl = sb("wl", [P, WC])
        wr = sb("wr", [P, RING, CHUNKS, WC])
        fsq = sb("fsq", [P, 1 + GROUPS * CHUNKS, EMB])
        fsql = sb("fsql", [P, EMB])
        sq = sb("sq", [P, SQ, CHUNKS, B])
        sqf = sb("sqf", [P, B])
        acc = sb("acc", [P, 2, B])
        prod = sb("prod", [P, B])
        pr = sb("pr", [P, C_ALL])
        bias = sb("bias", [P, 1])
        zero = sb("zero", [P, HALF], BF16)
        lin = sb("lin", [P, HALF])
        sqs = sb("sqs", [P, HALF])
        h1 = sb("h1", [P, 2, HALF])
        h2 = sb("h2", [P, HALF])
        gsq = sb("gsq", [P, QUART])
        z = sb("z", [P, QUART])
        sg = sb("sg", [P, QUART])
        y = sb("y", [P, QUART])
        warm = sb("warm", [P, 1])

        p_lin = bank("p_lin")
        p_sq = bank("p_sq")
        p_h1 = [bank("p_h1a"), bank("p_h1b")]
        p_h2 = bank("p_h2")
        p_tot = bank("p_tot")
        p_es = bank("p_es")

        first_landed = sem("first_landed")
        x_landed = [sem(f"x_landed{s}") for s in range(RING)]
        last_landed = sem("last_landed")
        w_landed = sem("w_landed")
        wl_landed = sem("wl_landed")
        pr_landed = sem("pr_landed")
        y_stored = sem("y_stored")
        zero_set = sem("zero_set")
        acc_set = sem("acc_set")
        fsq_ready = sem("fsq_ready")
        s_ready = sem("s_ready")
        bias_ready = sem("bias_ready")
        wr_ready = sem("wr_ready")
        squared = sem("squared")
        sqf_ready = sem("sqf_ready")
        added = sem("added")
        lin_used = sem("lin_used")
        sq_used = sem("sq_used")
        prod_ready = sem("prod_ready")
        p_lin_done = sem("p_lin_done")
        lin_ready = sem("lin_ready")
        sqs_ready = sem("sqs_ready")
        p_h1_done = sem("p_h1_done")
        h1a_ready = sem("h1a_ready")
        h1b_ready = sem("h1b_ready")
        p_h2_done = sem("p_h2_done")
        h2a_ready = sem("h2a_ready")
        h2b_ready = sem("h2b_ready")
        p_es_done = sem("p_es_done")
        gsq_ready = sem("gsq_ready")
        p_tot_done = sem("p_tot_done")
        z_ready = sem("z_ready")
        sg_ready = sem("sg_ready")
        y_ready = sem("y_ready")

        block = ctx.enter_context(nc.Block())

        def group(r, s):
            return RING * r + s

        def adds_by(r, s):
            return 1 + DVE_PER_PAIR * (RING // 2) * r + DVE_PER_PAIR * (s // 2) + (CHUNKS if s % 2 == 0 else DVE_PER_PAIR)

        @block.sync
        def _(sp):
            sp.dma_start(xf[:, :], x_first).then_inc(first_landed, 16)
            for s in range(RING):
                sp.dma_start(xr[:, s].rearrange("p c b -> p (c b)"), x_groups[s]).then_inc(x_landed[s], 16)
            with sp.Fori(1, ROUNDS) as r:
                for s in range(RING):
                    sp.wait_ge(lin_used, group(r - 1, s) + 1)
                    sp.wait_ge(squared, group(r - 1, s) + 1)
                    sp.dma_start(xr[:, s].rearrange("p c b -> p (c b)"),
                                 x_groups[bass.ds(group(r, s), 1)].rearrange("g p n -> (g p) n")
                                 ).then_inc(x_landed[s], 16)
            sp.dma_start(xl[0:LAST, :], x_last).then_inc(last_landed, 16)
            sp.wait_ge(y_ready, 1)
            sp.dma_start(out_rows, y[0:P:32, :]).then_inc(y_stored, 16)
            sp.wait_ge(y_stored, 16)

        @block.gpsimd
        def _(pool):
            def place(r, s):
                nc.gpsimd.tensor_copy(
                    wr[:, s].rearrange("p c k -> p (c k)"),
                    w[:, bass.ds(1 + CHUNKS * group(r, s), CHUNKS), :].rearrange("p c k -> p (c k)")
                ).then_inc(wr_ready, 1)

            pool.wait_ge(s_ready, 1)
            for s in range(RING):
                place(0, s)
            with pool.Fori(1, ROUNDS) as r:
                for s in range(RING):
                    pool.wait_ge(lin_used, group(r - 1, s) + 1)
                    if s % 2 == 1:
                        pool.wait_ge(sq_used, (RING // 2) * (r - 1) + s // 2 + 1)
                    pool.wait_ge(added, adds_by(r - 1, s))
                    place(r, s)

        @block.scalar
        def _(act):
            act.dma_start(w[:, :, :].rearrange("p c k -> p (c k)"), w_all).then_inc(w_landed, 16)
            act.dma_start(wl[0:LAST, :], w_last).then_inc(wl_landed, 16)
            act.dma_start(pr[:, :], params).then_inc(pr_landed, 16)
            act.wait_ge(zero_set, 1)
            nc.scalar.activation(warm[:, :], zero[:, 0:1], ACT.Sigmoid)
            act.wait_ge(first_landed, 16)
            nc.scalar.activation(sqf[:, :], xf[:, :], ACT.Square).then_inc(sqf_ready, 1)

            def square(r, s, waits):
                act.wait_ge(x_landed[s], 16 * (r + 1))
                if waits:
                    act.wait_ge(added, adds_by(r, s - SQ))
                    if s % 2 == 1:
                        act.wait_ge(sq_used, (RING // 2) * r + s // 2 - SQ // 2 + 1)
                nc.scalar.activation(sq[:, s % SQ].rearrange("p c b -> p (c b)"),
                                     xr[:, s].rearrange("p c b -> p (c b)"), ACT.Square).then_inc(squared, 1)

            for s in range(RING):
                square(0, s, s >= SQ)
            with act.Fori(1, ROUNDS) as r:
                for s in range(RING):
                    square(r, s, True)

            act.wait_ge(p_lin_done, 1)
            nc.scalar.copy(lin[:, :], p_lin[:, :]).then_inc(lin_ready, 1)
            act.wait_ge(pr_landed, 16)
            act.wait_ge(p_h1_done, 1)
            nc.scalar.activation(h1[:, 0, :], p_h1[0][:, :], ACT.Relu, bias=pr[:, C_B1:C_B1 + 1]).then_inc(h1a_ready, 1)
            act.wait_ge(p_es_done, 1)
            nc.scalar.activation(gsq[:, :], p_es[:, 0:QUART], ACT.Square).then_inc(gsq_ready, 1)
            act.wait_ge(p_h2_done, 1)
            nc.scalar.activation(h2[0:H2, :], p_h2[0:H2, :], ACT.Relu,
                                 bias=pr[0:H2, C_B2:C_B2 + 1]).then_inc(h2a_ready, 1)
            act.wait_ge(bias_ready, 1)
            act.wait_ge(z_ready, 1)
            nc.scalar.activation(sg[:, :], z[:, :], ACT.Sigmoid, bias=bias[:, :]).then_inc(sg_ready, 1)

        @block.vector
        def _(dve):
            nc.vector.memset(zero[:, :], 0.0).then_inc(zero_set, 1)
            nc.vector.memset(acc[:, :, :], 0.0).then_inc(acc_set, 1)
            dve.wait_ge(w_landed, 16)
            nc.vector.tensor_tensor(fsq[:, :, :], w[:, :, 0:EMB], w[:, :, 0:EMB], ALU.mult).then_inc(fsq_ready, 1)
            dve.wait_ge(wl_landed, 16)
            nc.vector.tensor_tensor(fsql[0:LAST, :], wl[0:LAST, 0:EMB], wl[0:LAST, 0:EMB],
                                    ALU.mult).then_inc(fsq_ready, 1)
            dve.wait_ge(fsq_ready, 1)
            nc.vector.tensor_reduce(w[:, :, LIN:WC], fsq[:, :, :], AX.X, ALU.add).then_inc(s_ready, 1)
            dve.wait_ge(fsq_ready, 2)
            nc.vector.tensor_reduce(wl[0:LAST, LIN:WC], fsql[0:LAST, :], AX.X, ALU.add).then_inc(s_ready, 1)
            dve.wait_ge(pr_landed, 16)
            nc.vector.tensor_tensor(bias[:, :], pr[:, C_BLIN:C_BLIN + 1], pr[:, C_B3:C_B3 + 1],
                                    ALU.add).then_inc(bias_ready, 1)

            dve.wait_ge(acc_set, 1)
            dve.wait_ge(s_ready, 1)
            dve.wait_ge(sqf_ready, 1)
            nc.vector.scalar_tensor_tensor(acc[:, 0, :], sqf[:, :], w[:, 0, LIN:WC], acc[:, 0, :],
                                           ALU.mult, ALU.add).then_inc(added, 1)

            def add(r, s):
                dve.wait_ge(squared, group(r, s) + 1)
                dve.wait_ge(wr_ready, group(r, s) + 1)
                chunks = CHUNKS if s % 2 == 0 else CHUNKS - 1
                for c in range(chunks):
                    before = adds_by(r, s) - chunks + c
                    turn = (1 + DVE_PER_PAIR * (s // 2) + CHUNKS * (s % 2) + c) % 2
                    if type(before) is not int or before > 1:
                        dve.wait_ge(added, before - 1)
                    nc.vector.scalar_tensor_tensor(acc[:, turn, :], sq[:, s % SQ, c, :], wr[:, s, c, LIN:WC],
                                                   acc[:, turn, :], ALU.mult, ALU.add).then_inc(added, 1)

            for s in range(RING):
                add(0, s)
            with dve.Fori(1, ROUNDS) as r:
                for s in range(RING):
                    add(r, s)

            dve.wait_ge(last_landed, 16)
            dve.wait_ge(s_ready, 2)
            nc.vector.scalar_tensor_tensor(prod[0:LAST, :], xl[0:LAST, :], wl[0:LAST, LIN:WC], xl[0:LAST, :],
                                           ALU.mult, ALU.mult).then_inc(prod_ready, 1)
            dve.wait_ge(sq_used, GROUPS // 2)
            nc.vector.tensor_copy(sqs[:, :], p_sq[:, :]).then_inc(sqs_ready, 1)
            dve.wait_ge(p_h1_done, 2)
            nc.vector.tensor_scalar(h1[:, 1, :], p_h1[1][:, :], pr[:, C_B1:C_B1 + 1], 0.0,
                                    ALU.add, ALU.max).then_inc(h1b_ready, 1)
            dve.wait_ge(p_h2_done, 2)
            nc.vector.tensor_scalar(h2[H2:P, :], p_h2[H2:P, :], pr[H2:P, C_B2:C_B2 + 1], 0.0,
                                    ALU.add, ALU.max).then_inc(h2b_ready, 1)
            dve.wait_ge(gsq_ready, 1)
            dve.wait_ge(p_tot_done, 1)
            nc.vector.scalar_tensor_tensor(z[:, :], gsq[:, :], 0.5, p_tot[:, 0:QUART],
                                           ALU.mult, ALU.add).then_inc(z_ready, 1)
            dve.wait_ge(sg_ready, 1)
            nc.vector.tensor_scalar(y[:, :], sg[:, :], 5.0, 0.5, ALU.mult, ALU.add).then_inc(y_ready, 1)

        @block.tensor
        def _(pe):
            def tile_mm(ps, tile, rows, width, lhsT, rhs):
                return nc.tensor.matmul(ps[32 * tile:32 * tile + rows, 0:width], lhsT, rhs,
                                        start=False, stop=False, skip_group_check=True)

            pe.wait_ge(zero_set, 1)
            for ps in (p_lin, p_sq, p_tot, p_es):
                nc.tensor.matmul(ps[:, :], zero[:, 0:P], zero[:, :], start=True, stop=False, skip_group_check=True)

            pe.wait_ge(first_landed, 16)
            pe.wait_ge(w_landed, 16)
            for h in range(2):
                tile_mm(p_lin, h, LIN, HALF, w[:, 0, 0:LIN], xf[:, h * HALF:(h + 1) * HALF])

            def multiply(r, s):
                pe.wait_ge(x_landed[s], 16 * (r + 1))
                pe.wait_ge(wr_ready, group(r, s) + 1)
                for c in range(CHUNKS):
                    for h in range(2):
                        mm = tile_mm(p_lin, 2 * (c % 2) + h, LIN, HALF, wr[:, s, c, 0:LIN],
                                     xr[:, s, c, h * HALF:(h + 1) * HALF])
                mm.then_inc(lin_used, 1)
                if s % 2 == 1:
                    pe.wait_ge(squared, group(r, s) + 1)
                    c = CHUNKS - 1
                    for h in range(2):
                        mm = tile_mm(p_sq, 2 * (s // 2 % 2) + h, 1, HALF, wr[:, s, c, LIN:WC],
                                     sq[:, s % SQ, c, h * HALF:(h + 1) * HALF])
                    mm.then_inc(sq_used, 1)

            for s in range(RING):
                multiply(0, s)
            with pe.Fori(1, ROUNDS) as r:
                for s in range(RING):
                    multiply(r, s)

            pe.wait_ge(last_landed, 16)
            pe.wait_ge(wl_landed, 16)
            for u in range(2):
                for h in range(2):
                    b0 = h * HALF + u * QUART
                    mm = nc.tensor.matmul(p_lin[32 * (2 * u + h):32 * (2 * u + h) + LIN, u * QUART:(u + 1) * QUART],
                                          wl[0:LAST, 0:LIN], xl[0:LAST, b0:b0 + QUART],
                                          start=False, stop=False, skip_group_check=True)
            mm.then_inc(p_lin_done, 1)

            def col(i):
                return pr[:, i:i + 1]

            def quarters(ps, lhsT, rhs):
                for h in range(2):
                    for u in range(2):
                        mm = tile_mm(ps, 2 * h + u, 1, QUART, lhsT(h), rhs(h, u))
                return mm

            pe.wait_ge(pr_landed, 16)
            pe.wait_ge(lin_ready, 1)
            for h in range(2):
                nc.tensor.matmul(p_h1[h][:, :], pr[:, C_W1 + h * H1:C_W1 + (h + 1) * H1], lin[:, :],
                                 start=True, stop=True).then_inc(p_h1_done, 1)
            quarters(p_es, lambda h: col(C_SE + h), lambda h, u: lin[:, u * QUART:(u + 1) * QUART]).then_inc(p_es_done, 1)
            quarters(p_tot, lambda h: col(C_SX + h), lambda h, u: lin[:, u * QUART:(u + 1) * QUART])
            pe.wait_ge(h1a_ready, 1)
            nc.tensor.matmul(p_h2[0:H2, :], pr[:, C_W2:C_W2 + H2], h1[:, 0, :], start=True, stop=True).then_inc(p_h2_done, 1)
            pe.wait_ge(h1b_ready, 1)
            nc.tensor.matmul(p_h2[H2:P, :], pr[:, C_W2:C_W2 + H2], h1[:, 1, :], start=True, stop=True).then_inc(p_h2_done, 1)
            pe.wait_ge(added, 1 + DVE_PER_PAIR * GROUPS // 2)
            for turn in range(2):
                quarters(p_tot, lambda h: col(C_NH),
                         lambda h, u: acc[:, turn, h * HALF + u * QUART:h * HALF + (u + 1) * QUART])
            pe.wait_ge(prod_ready, 1)
            quarters(p_tot, lambda h: pr[0:LAST, C_NH:C_NH + 1],
                     lambda h, u: prod[0:LAST, h * HALF + u * QUART:h * HALF + (u + 1) * QUART])
            pe.wait_ge(sqs_ready, 1)
            quarters(p_tot, lambda h: col(C_SS + h), lambda h, u: sqs[:, u * QUART:(u + 1) * QUART])
            pe.wait_ge(h2a_ready, 1)
            pe.wait_ge(h2b_ready, 1)
            quarters(p_tot, lambda h: col(C_W3 + h), lambda h, u: h2[:, u * QUART:(u + 1) * QUART]).then_inc(p_tot_done, 1)


def kernel(r_input_data, L0_rec_W_lin, L0_rec_b_lin, L0_rec_factors, L0_rec_W1, L0_rec_b1, L0_rec_W2, L0_rec_b2,
           L0_rec_W3, L0_rec_b3):
    import numpy as np
    import concourse.bacc as bacc
    from concourse.bass_utils import run_bass_kernel_spmd

    f32 = np.float32
    xT = np.ascontiguousarray(np.asarray(r_input_data).T)
    wrow = np.concatenate([np.asarray(L0_rec_factors), np.asarray(L0_rec_W_lin).T, np.zeros((N, 1), f32)], axis=1)
    w_groups = wrow[P:N - LAST].reshape(GROUPS, P, CHUNKS * WC).transpose(1, 0, 2).reshape(P, -1)
    w_all = np.ascontiguousarray(np.concatenate([wrow[:P], w_groups], axis=1))
    w_last = np.ascontiguousarray(wrow[N - LAST:])

    params = np.zeros((P, C_ALL), f32)
    for t in range(4):
        h = t % 2
        params[32 * t:32 * t + EMB, C_W1 + h * H1:C_W1 + (h + 1) * H1] = np.asarray(L0_rec_W1).T
        params[32 * t:32 * t + EMB, C_SE + h] = 1.0
        params[32 * t + EMB, C_SX + h] = 1.0
        params[32 * t, C_SS + h] = -0.5
    params[:, C_W2:C_W2 + H2] = np.asarray(L0_rec_W2).T
    params[:, C_B1] = np.asarray(L0_rec_b1)
    for h in range(2):
        params[h * H2:(h + 1) * H2, C_B2] = np.asarray(L0_rec_b2)
        params[h * H2:(h + 1) * H2, C_W3 + h] = np.asarray(L0_rec_W3)[0]
    params[:, C_BLIN] = np.asarray(L0_rec_b_lin)
    params[:, C_B3] = np.asarray(L0_rec_b3)
    params[:, C_NH] = -0.5

    arrays = {"xT": xT, "w_all": w_all, "w_last": w_last, "params": params}
    nc = bacc.Bacc("TRN2", target_bir_lowering=False, num_devices=1)
    args = [nc.dram_tensor(f"in_{name}", a.shape, F32, kind="ExternalInput").ap() for name, a in arrays.items()]
    out = nc.dram_tensor("out_y", (B,), F32, kind="ExternalOutput").ap()
    fm_kernel(nc, *args, out)
    r = run_bass_kernel_spmd(nc, [{f"in_{name}": a for name, a in arrays.items()}], core_ids=[0])
    return r.results[0]["out_y"]
```

```python
from contextlib import ExitStack

import concourse.bass as bass
from concourse import mybir

ALU = mybir.AluOpType
ACT = mybir.ActivationFunctionType
AX = mybir.AxisListType
F32 = mybir.dt.float32
BF16 = mybir.dt.bfloat16

B, N, EMB = 1024, 12500, 16
H1, H2 = 128, 64
P = 128

CHUNKS = 2
RING = 8
GROUPS = (N - P) // (P * CHUNKS)
ROUNDS = GROUPS // RING
LAST = N - P - GROUPS * P * CHUNKS
assert ROUNDS * RING == GROUPS and 0 < LAST <= P and RING % 4 == 0

LIN = EMB + 1
WC = LIN + 1

HALF = B // 2
QUART = HALF // 2
SQ = 4
DVE_PER_PAIR = 2 * CHUNKS - 1

C_W1 = 0
C_W2 = C_W1 + 2 * H1
C_B1 = C_W2 + H2
C_B2 = C_B1 + 1
C_W3 = C_B2 + 1
C_BLIN = C_W3 + 2
C_B3 = C_BLIN + 1
C_SX = C_B3 + 1
C_SE = C_SX + 2
C_SS = C_SE + 2
C_ONE = C_SS + 2
C_ALL = C_ONE + 1


def fm_kernel(nc, xT, w_all, w_last, params, out):
    x_first = xT[0:P, :]
    x_groups = xT[P:P + GROUPS * P * CHUNKS, :].rearrange("(g p c) b -> g p (c b)", p=P, c=CHUNKS)
    x_last = xT[N - LAST:N, :]
    out_rows = out.rearrange("(q b) -> q b", b=QUART)

    with ExitStack() as ctx:
        def sb(name, shape, dt=F32):
            return ctx.enter_context(nc.sbuf_tensor(name, shape, dt))

        def bank(name):
            return ctx.enter_context(nc.psum_tensor(name, [P, HALF], F32))

        def sem(name):
            return ctx.enter_context(nc.semaphore(name))

        xf = sb("xf", [P, B])
        xr = sb("xr", [P, RING, CHUNKS, B])
        xl = sb("xl", [P, B])
        w = sb("w", [P, 1 + GROUPS * CHUNKS, WC])
        wl = sb("wl", [P, WC])
        wr = sb("wr", [P, RING, CHUNKS, WC])
        fsq = sb("fsq", [P, 1 + GROUPS * CHUNKS, EMB])
        fsql = sb("fsql", [P, EMB])
        sq = sb("sq", [P, SQ, CHUNKS, B])
        sqf = sb("sqf", [P, B])
        acc = sb("acc", [P, B])
        prod = sb("prod", [P, B])
        xlsq = sb("xlsq", [P, B])
        pr = sb("pr", [P, C_ALL])
        bias = sb("bias", [P, 1])
        zero = sb("zero", [P, HALF], BF16)
        lin = sb("lin", [P, 2, QUART])
        sqs = sb("sqs", [P, HALF])
        h1 = sb("h1", [P, 2, 2, QUART])
        h2 = sb("h2", [P, 2, QUART])
        gsq = sb("gsq", [P, QUART])
        z = sb("z", [P, QUART])
        sg = sb("sg", [P, QUART])
        y = sb("y", [P, QUART])
        warm = sb("warm", [P, 1])

        p_lin = bank("p_lin")
        p_sq = bank("p_sq")
        p_h1 = [[bank(f"p_h1{h}{u}") for u in range(2)] for h in range(2)]
        p_h2 = [bank("p_h2"), p_sq]
        p_tot = bank("p_tot")

        first_landed = sem("first_landed")
        x_landed = [sem(f"x_landed{s}") for s in range(RING)]
        last_landed = sem("last_landed")
        w_landed = sem("w_landed")
        wl_landed = sem("wl_landed")
        pr_landed = sem("pr_landed")
        y_stored = sem("y_stored")
        zero_set = sem("zero_set")
        acc_set = sem("acc_set")
        fsq_ready = sem("fsq_ready")
        s_ready = sem("s_ready")
        bias_ready = sem("bias_ready")
        wr_ready = sem("wr_ready")
        squared = sem("squared")
        sqf_ready = sem("sqf_ready")
        added = sem("added")
        lin_used = sem("lin_used")
        sq_used = sem("sq_used")
        prod_ready = sem("prod_ready")
        xlsq_ready = sem("xlsq_ready")
        p_lin_done = sem("p_lin_done")
        lin_ready = sem("lin_ready")
        sqs_ready = sem("sqs_ready")
        p_h1_done = sem("p_h1_done")
        h1a_ready = sem("h1a_ready")
        h1b_ready = sem("h1b_ready")
        p_h2_done = sem("p_h2_done")
        h2a_ready = sem("h2a_ready")
        h2b_ready = sem("h2b_ready")
        p_es_done = sem("p_es_done")
        gsq_ready = sem("gsq_ready")
        p_tot_done = sem("p_tot_done")
        z_ready = sem("z_ready")
        sg_ready = sem("sg_ready")
        y_ready = sem("y_ready")

        block = ctx.enter_context(nc.Block())

        def last_group(r, s):
            return type(r) is int and group(r, s) == GROUPS - 1

        def group(r, s):
            return RING * r + s

        def pair(r, s):
            return (RING // 2) * r + s // 2

        def squares_by(r, s, c):
            return CHUNKS * group(r, s) + c + 1

        def adds_by(r, s):
            return 1 + DVE_PER_PAIR * pair(r, s) + (CHUNKS if s % 2 == 0 else DVE_PER_PAIR)

        ADDS = adds_by(ROUNDS - 1, RING - 2)
        PAIRS = GROUPS // 2 - 1

        @block.sync
        def _(sp):
            sp.dma_start(xf[:, :], x_first).then_inc(first_landed, 16)
            for s in range(RING):
                sp.dma_start(xr[:, s].rearrange("p c b -> p (c b)"), x_groups[s]).then_inc(x_landed[s], 16)
            with sp.Fori(1, ROUNDS) as r:
                for s in range(RING):
                    sp.wait_ge(lin_used, group(r - 1, s) + 1)
                    sp.wait_ge(squared, squares_by(r - 1, s, CHUNKS - 1))
                    sp.dma_start(xr[:, s].rearrange("p c b -> p (c b)"),
                                 x_groups[bass.ds(group(r, s), 1)].rearrange("g p n -> (g p) n")
                                 ).then_inc(x_landed[s], 16)
            sp.dma_start(xl[0:LAST, :], x_last).then_inc(last_landed, 16)
            sp.wait_ge(y_ready, 1)
            sp.dma_start(out_rows, y[0:P:32, :]).then_inc(y_stored, 16)
            sp.wait_ge(y_stored, 16)

        @block.gpsimd
        def _(pool):
            def place(r, s):
                nc.gpsimd.tensor_copy(
                    wr[:, s].rearrange("p c k -> p (c k)"),
                    w[:, bass.ds(1 + CHUNKS * group(r, s), CHUNKS), :].rearrange("p c k -> p (c k)")
                ).then_inc(wr_ready, 1)

            pool.wait_ge(s_ready, 1)
            for s in range(RING):
                place(0, s)
            with pool.Fori(1, ROUNDS) as r:
                for s in range(RING):
                    pool.wait_ge(lin_used, group(r - 1, s) + 1)
                    if s % 2 == 1:
                        pool.wait_ge(sq_used, pair(r - 1, s) + 1)
                    pool.wait_ge(added, adds_by(r - 1, s))
                    place(r, s)
            pool.wait_ge(last_landed, 16)
            nc.gpsimd.tensor_tensor(xlsq[0:LAST, :], xl[0:LAST, :], xl[0:LAST, :], ALU.mult).then_inc(xlsq_ready, 1)

        @block.scalar
        def _(act):
            act.dma_start(w[:, :, :].rearrange("p c k -> p (c k)"), w_all).then_inc(w_landed, 16)
            act.dma_start(wl[0:LAST, :], w_last).then_inc(wl_landed, 16)
            act.dma_start(pr[:, :], params).then_inc(pr_landed, 16)
            act.wait_ge(zero_set, 1)
            nc.scalar.activation(warm[:, :], zero[:, 0:1], ACT.Sigmoid)
            act.wait_ge(first_landed, 16)
            nc.scalar.activation(sqf[:, :], xf[:, :], ACT.Square).then_inc(sqf_ready, 1)

            def square(r, s):
                act.wait_ge(x_landed[s], 16 * (r + 1))
                if type(r) is not int or group(r, s) >= SQ:
                    act.wait_ge(added, adds_by(r, s - SQ))
                    if s % 2 == 1:
                        act.wait_ge(sq_used, pair(r, s - SQ) + 1)
                for c in range(CHUNKS):
                    if last_group(r, s) and c < CHUNKS - 1:
                        continue
                    nc.scalar.activation(sq[:, s % SQ, c, :], xr[:, s, c, :], ACT.Square).then_inc(squared, 1)

            for s in range(RING):
                square(0, s)
            with act.Fori(1, ROUNDS - 1) as r:
                for s in range(RING):
                    square(r, s)
            for s in range(RING - 1):
                square(ROUNDS - 1, s)
            act.wait_ge(sq_used, PAIRS)
            nc.scalar.copy(sqs[:, :], p_sq[:, :]).then_inc(sqs_ready, 1)
            square(ROUNDS - 1, RING - 1)

            act.wait_ge(p_lin_done, 1)
            for u in range(2):
                nc.scalar.copy(lin[:, u, :], p_lin[:, u * QUART:(u + 1) * QUART]).then_inc(lin_ready, 1)
            act.wait_ge(pr_landed, 16)
            for u in range(2):
                act.wait_ge(p_h1_done, 2 * u + 1)
                nc.scalar.activation(h1[:, 0, u, :], p_h1[0][u][:, 0:QUART], ACT.Relu,
                                     bias=pr[:, C_B1:C_B1 + 1]).then_inc(h1a_ready, 1)
            act.wait_ge(p_es_done, 1)
            nc.scalar.activation(gsq[:, :], p_lin[:, 0:QUART], ACT.Square).then_inc(gsq_ready, 1)
            act.wait_ge(p_h2_done, 1)
            nc.scalar.activation(h2[:, 0, :], p_h2[0][:, 0:QUART], ACT.Relu,
                                 bias=pr[:, C_B2:C_B2 + 1]).then_inc(h2a_ready, 1)
            act.wait_ge(bias_ready, 1)
            act.wait_ge(z_ready, 1)
            nc.scalar.activation(sg[:, :], z[:, :], ACT.Sigmoid, bias=bias[:, :]).then_inc(sg_ready, 1)

        @block.vector
        def _(dve):
            nc.vector.memset(zero[:, :], 0.0).then_inc(zero_set, 1)
            nc.vector.memset(acc[:, :], 0.0).then_inc(acc_set, 1)
            dve.wait_ge(w_landed, 16)
            nc.vector.scalar_tensor_tensor(fsq[:, :, :], w[:, :, 0:EMB], -0.5, w[:, :, 0:EMB],
                                           ALU.mult, ALU.mult).then_inc(fsq_ready, 1)
            dve.wait_ge(wl_landed, 16)
            nc.vector.scalar_tensor_tensor(fsql[0:LAST, :], wl[0:LAST, 0:EMB], -0.5, wl[0:LAST, 0:EMB],
                                           ALU.mult, ALU.mult).then_inc(fsq_ready, 1)
            dve.wait_ge(fsq_ready, 1)
            nc.vector.tensor_reduce(w[:, :, LIN:WC], fsq[:, :, :], AX.X, ALU.add).then_inc(s_ready, 1)
            dve.wait_ge(fsq_ready, 2)
            nc.vector.tensor_reduce(wl[0:LAST, LIN:WC], fsql[0:LAST, :], AX.X, ALU.add).then_inc(s_ready, 1)
            dve.wait_ge(pr_landed, 16)
            nc.vector.tensor_tensor(bias[:, :], pr[:, C_BLIN:C_BLIN + 1], pr[:, C_B3:C_B3 + 1],
                                    ALU.add).then_inc(bias_ready, 1)

            dve.wait_ge(acc_set, 1)
            dve.wait_ge(s_ready, 1)
            dve.wait_ge(sqf_ready, 1)
            nc.vector.scalar_tensor_tensor(acc[:, :], sqf[:, :], w[:, 0, LIN:WC], acc[:, :],
                                           ALU.mult, ALU.add).then_inc(added, 1)

            def add(r, s):
                dve.wait_ge(wr_ready, group(r, s) + 1)
                chunks = CHUNKS if s % 2 == 0 else CHUNKS - 1
                for c in range(chunks):
                    dve.wait_ge(squared, squares_by(r, s, c))
                    dve.wait_ge(added, adds_by(r, s) - chunks + c)
                    nc.vector.scalar_tensor_tensor(acc[:, :], sq[:, s % SQ, c, :], wr[:, s, c, LIN:WC],
                                                   acc[:, :], ALU.mult, ALU.add).then_inc(added, 1)

            for s in range(RING):
                add(0, s)
            with dve.Fori(1, ROUNDS - 1) as r:
                for s in range(RING):
                    add(r, s)
            for s in range(RING - 1):
                add(ROUNDS - 1, s)

            dve.wait_ge(x_landed[RING - 1], 16 * ROUNDS)
            dve.wait_ge(wr_ready, GROUPS)
            nc.vector.scalar_tensor_tensor(prod[:, :], xr[:, RING - 1, 0, :], wr[:, RING - 1, 0, LIN:WC],
                                           xr[:, RING - 1, 0, :], ALU.mult, ALU.mult).then_inc(prod_ready, 1)
            for u in range(2):
                dve.wait_ge(p_h1_done, 2 * u + 2)
                nc.vector.tensor_scalar(h1[:, 1, u, :], p_h1[1][u][:, 0:QUART], pr[:, C_B1:C_B1 + 1], 0.0,
                                        ALU.add, ALU.max).then_inc(h1b_ready, 1)
            dve.wait_ge(p_h2_done, 2)
            nc.vector.tensor_scalar(h2[:, 1, :], p_h2[1][:, 0:QUART], pr[:, C_B2:C_B2 + 1], 0.0,
                                    ALU.add, ALU.max).then_inc(h2b_ready, 1)
            dve.wait_ge(gsq_ready, 1)
            dve.wait_ge(p_tot_done, 1)
            nc.vector.scalar_tensor_tensor(z[:, :], gsq[:, :], 0.5, p_tot[:, 0:QUART],
                                           ALU.mult, ALU.add).then_inc(z_ready, 1)
            dve.wait_ge(sg_ready, 1)
            nc.vector.tensor_scalar(y[:, :], sg[:, :], 5.0, 0.5, ALU.mult, ALU.add).then_inc(y_ready, 1)

        @block.tensor
        def _(pe):
            def add_mm(out, lhsT, rhs):
                return nc.tensor.matmul(out, lhsT, rhs, start=False, stop=False, skip_group_check=True)

            def tile_rows(ps, tile, rows, width=HALF):
                return ps[32 * tile:32 * tile + rows, 0:width]

            pe.wait_ge(zero_set, 1)
            for ps in (p_lin, p_sq, p_tot):
                nc.tensor.matmul(ps[:, :], zero[:, 0:P], zero[:, :], start=True, stop=False, skip_group_check=True)

            pe.wait_ge(first_landed, 16)
            pe.wait_ge(w_landed, 16)
            for h in range(2):
                add_mm(tile_rows(p_lin, h, LIN), w[:, 0, 0:LIN], xf[:, h * HALF:(h + 1) * HALF])

            def squares_of_pair(r, s):
                pe.wait_ge(squared, squares_by(r, s, CHUNKS - 1))
                c, s = CHUNKS - 1, s % RING
                for h in range(2):
                    mm = add_mm(tile_rows(p_sq, 2 * (s // 2 % 2) + h, 1), wr[:, s, c, LIN:WC],
                                sq[:, s % SQ, c, h * HALF:(h + 1) * HALF])
                mm.then_inc(sq_used, 1)

            def multiply(r, s):
                pe.wait_ge(x_landed[s], 16 * (r + 1))
                pe.wait_ge(wr_ready, group(r, s) + 1)
                for c in range(CHUNKS):
                    for h in range(2):
                        mm = add_mm(tile_rows(p_lin, 2 * (c % 2) + h, LIN), wr[:, s, c, 0:LIN],
                                    xr[:, s, c, h * HALF:(h + 1) * HALF])
                mm.then_inc(lin_used, 1)
                if s % 2 == 0 and not (type(r) is int and group(r, s) == 0):
                    squares_of_pair(r, s - 1)

            for s in range(RING):
                multiply(0, s)
            with pe.Fori(1, ROUNDS - 1) as r:
                for s in range(RING):
                    multiply(r, s)
            for s in range(RING):
                multiply(ROUNDS - 1, s)

            def col(i, rows=P):
                return pr[0:rows, i:i + 1]

            def quarter(h, u):
                return slice(h * HALF + u * QUART, h * HALF + (u + 1) * QUART)

            def quarters(ps, lhsT, rhs, add=True):
                for h in range(2):
                    for u in range(2):
                        mm = nc.tensor.matmul(tile_rows(ps, 2 * h + u, 1, QUART), lhsT(h), rhs(h, u),
                                              start=not add, stop=not add, skip_group_check=True)
                return mm

            pe.wait_ge(pr_landed, 16)
            pe.wait_ge(sqs_ready, 1)
            quarters(p_tot, lambda h: col(C_SS + h), lambda h, u: sqs[:, u * QUART:(u + 1) * QUART])
            pe.wait_ge(added, ADDS)
            quarters(p_tot, lambda h: col(C_ONE), lambda h, u: acc[:, quarter(h, u)])
            pe.wait_ge(squared, CHUNKS * GROUPS - 1)
            quarters(p_tot, lambda h: wr[:, RING - 1, CHUNKS - 1, LIN:WC],
                     lambda h, u: sq[:, (RING - 1) % SQ, CHUNKS - 1, quarter(h, u)])

            pe.wait_ge(last_landed, 16)
            pe.wait_ge(wl_landed, 16)
            for u in range(2):
                for h in range(2):
                    t = 2 * u + h
                    mm = add_mm(p_lin[32 * t:32 * t + LIN, u * QUART:(u + 1) * QUART], wl[0:LAST, 0:LIN],
                                xl[0:LAST, quarter(h, u)])
            mm.then_inc(p_lin_done, 1)
            pe.wait_ge(prod_ready, 1)
            quarters(p_tot, lambda h: col(C_ONE), lambda h, u: prod[:, quarter(h, u)])

            for u in range(2):
                pe.wait_ge(lin_ready, u + 1)
                for h in range(2):
                    nc.tensor.matmul(p_h1[h][u][:, 0:QUART], pr[:, C_W1 + h * H1:C_W1 + (h + 1) * H1], lin[:, u, :],
                                     start=True, stop=True).then_inc(p_h1_done, 1)
            quarters(p_lin, lambda h: col(C_SE + h), lambda h, u: lin[:, u, :], add=False).then_inc(p_es_done, 1)
            for u in range(2):
                pe.wait_ge(h1a_ready, u + 1)
                nc.tensor.matmul(p_h2[u][0:H2, 0:QUART], pr[:, C_W2:C_W2 + H2], h1[:, 0, u, :], start=True, stop=True)
                pe.wait_ge(h1b_ready, u + 1)
                nc.tensor.matmul(p_h2[u][H2:P, 0:QUART], pr[:, C_W2:C_W2 + H2], h1[:, 1, u, :],
                                 start=True, stop=True).then_inc(p_h2_done, 1)
            quarters(p_tot, lambda h: col(C_SX + h), lambda h, u: lin[:, u, :])
            pe.wait_ge(xlsq_ready, 1)
            pe.wait_ge(s_ready, 2)
            quarters(p_tot, lambda h: wl[0:LAST, LIN:WC], lambda h, u: xlsq[0:LAST, quarter(h, u)])
            pe.wait_ge(h2a_ready, 1)
            pe.wait_ge(h2b_ready, 1)
            quarters(p_tot, lambda h: col(C_W3 + h), lambda h, u: h2[:, u, :]).then_inc(p_tot_done, 1)


def kernel(r_input_data, L0_rec_W_lin, L0_rec_b_lin, L0_rec_factors, L0_rec_W1, L0_rec_b1, L0_rec_W2, L0_rec_b2,
           L0_rec_W3, L0_rec_b3):
    import numpy as np
    import concourse.bacc as bacc
    from concourse.bass_utils import run_bass_kernel_spmd

    f32 = np.float32
    xT = np.ascontiguousarray(np.asarray(r_input_data).T)
    wrow = np.concatenate([np.asarray(L0_rec_factors), np.asarray(L0_rec_W_lin).T, np.zeros((N, 1), f32)], axis=1)
    w_groups = wrow[P:N - LAST].reshape(GROUPS, P, CHUNKS * WC).transpose(1, 0, 2).reshape(P, -1)
    w_all = np.ascontiguousarray(np.concatenate([wrow[:P], w_groups], axis=1))
    w_last = np.ascontiguousarray(wrow[N - LAST:])

    params = np.zeros((P, C_ALL), f32)
    for t in range(4):
        h = t % 2
        params[32 * t:32 * t + EMB, C_W1 + h * H1:C_W1 + (h + 1) * H1] = np.asarray(L0_rec_W1).T
        params[32 * t:32 * t + EMB, C_SE + h] = 1.0
        params[32 * t + EMB, C_SX + h] = 1.0
        params[32 * t, C_SS + h] = 1.0
    params[:, C_W2:C_W2 + H2] = np.asarray(L0_rec_W2).T
    params[:, C_B1] = np.asarray(L0_rec_b1)
    for h in range(2):
        params[h * H2:(h + 1) * H2, C_B2] = np.asarray(L0_rec_b2)
        params[h * H2:(h + 1) * H2, C_W3 + h] = np.asarray(L0_rec_W3)[0]
    params[:, C_BLIN] = np.asarray(L0_rec_b_lin)
    params[:, C_B3] = np.asarray(L0_rec_b3)
    params[:, C_ONE] = 1.0

    arrays = {"xT": xT, "w_all": w_all, "w_last": w_last, "params": params}
    nc = bacc.Bacc("TRN2", target_bir_lowering=False, num_devices=1)
    args = [nc.dram_tensor(f"in_{name}", a.shape, F32, kind="ExternalInput").ap() for name, a in arrays.items()]
    out = nc.dram_tensor("out_y", (B,), F32, kind="ExternalOutput").ap()
    fm_kernel(nc, *args, out)
    r = run_bass_kernel_spmd(nc, [{f"in_{name}": a for name, a in arrays.items()}], core_ids=[0])
    return r.results[0]["out_y"]
```

```python
from contextlib import ExitStack

import concourse.bass as bass
from concourse import mybir

ALU = mybir.AluOpType
ACT = mybir.ActivationFunctionType
AX = mybir.AxisListType
F32 = mybir.dt.float32
BF16 = mybir.dt.bfloat16

B, N, EMB = 1024, 12500, 16
H1, H2 = 128, 64
P = 128

CHUNKS = 2
RING = 8
GROUPS = (N - P) // (P * CHUNKS)
ROUNDS = GROUPS // RING
LAST = N - P - GROUPS * P * CHUNKS
assert ROUNDS * RING == GROUPS and 0 < LAST <= P and RING % 4 == 0

LIN = EMB + 1
WC = LIN + 1

HALF = B // 2
QUART = HALF // 2
EIGHTH = QUART // 2
SQ = 4
END = 4
DVE_PER_PAIR = 2 * CHUNKS - 1

C_W1 = 0
C_W2 = C_W1 + H1
C_B1 = C_W2 + H2
C_B2 = C_B1 + 1
C_W3 = C_B2 + 1
C_BLIN = C_W3 + 2
C_B3 = C_BLIN + 1
C_SX = C_B3 + 1
C_SE = C_SX + 1
C_ONE = C_SE + 1
C_ALL = C_ONE + 1


def fm_kernel(nc, xT, w_all, w_last, params, out):
    x_first = xT[0:P, :]
    x_groups = xT[P:P + GROUPS * P * CHUNKS, :].rearrange("(g p c) b -> g p (c b)", p=P, c=CHUNKS)
    x_last = xT[N - LAST:N, :]
    out_rows = out.rearrange("(h t b) -> t h b", h=2, t=4)

    with ExitStack() as ctx:
        def sb(name, shape, dt=F32):
            return ctx.enter_context(nc.sbuf_tensor(name, shape, dt))

        def bank(name):
            return ctx.enter_context(nc.psum_tensor(name, [P, HALF], F32))

        def sem(name):
            return ctx.enter_context(nc.semaphore(name))

        xf = sb("xf", [P, B])
        xr = sb("xr", [P, RING, CHUNKS, B])
        xl = sb("xl", [P, B])
        w = sb("w", [P, 1 + GROUPS * CHUNKS, WC])
        wl = sb("wl", [P, WC])
        wr = sb("wr", [P, RING, CHUNKS, WC])
        fsq = sb("fsq", [P, 1 + GROUPS * CHUNKS, EMB])
        fsql = sb("fsql", [P, EMB])
        sq = sb("sq", [P, SQ, CHUNKS, B])
        sqf = sb("sqf", [P, B])
        acc = sb("acc", [P, B])
        prod = sb("prod", [P, B])
        pr = sb("pr", [P, C_ALL])
        bias = sb("bias", [P, 1])
        zero = sb("zero", [P, HALF], BF16)
        lin = sb("lin", [P, 2, 2, QUART])
        sqs = sb("sqs", [P, 2, HALF])
        h1 = sb("h1", [P, 2, 2, QUART])
        h2 = sb("h2", [P, 2, 2, QUART])
        gsq = sb("gsq", [P, QUART])
        z = sb("z", [P, QUART])
        sg = sb("sg", [P, QUART])
        y = sb("y", [P, QUART])
        warm = sb("warm", [P, 1])

        p_lin = [bank("p_lin0"), bank("p_lin1")]
        p_sq = bank("p_sq")
        p_h1 = [bank("p_h10"), bank("p_h11")]
        p_h2 = bank("p_h2")
        p_tot = bank("p_tot")
        p_es = bank("p_es")

        first_landed = sem("first_landed")
        x_landed = [sem(f"x_landed{s}") for s in range(RING)]
        end_landed = [[sem(f"end_landed{i}{h}") for h in range(2)] for i in range(END)]
        last_landed = [sem("last_landed0"), sem("last_landed1")]
        w_landed = sem("w_landed")
        wl_landed = sem("wl_landed")
        pr_landed = sem("pr_landed")
        y_stored = sem("y_stored")
        zero_set = sem("zero_set")
        acc_set = sem("acc_set")
        pads_set = sem("pads_set")
        fsq_ready = sem("fsq_ready")
        s_ready = sem("s_ready")
        bias_ready = sem("bias_ready")
        wr_ready = sem("wr_ready")
        squared = sem("squared")
        sqf_ready = sem("sqf_ready")
        added = sem("added")
        lin_used = sem("lin_used")
        sq_used = sem("sq_used")
        prod_ready = sem("prod_ready")
        p_lin_done = sem("p_lin_done")
        lin_ready = sem("lin_ready")
        sqs_ready = sem("sqs_ready")
        p_h1_done = sem("p_h1_done")
        h1a_ready = sem("h1a_ready")
        h1b_ready = sem("h1b_ready")
        p_h2_done = sem("p_h2_done")
        h2a_ready = sem("h2a_ready")
        h2b_ready = sem("h2b_ready")
        p_es_done = sem("p_es_done")
        gsq_ready = sem("gsq_ready")
        p_tot_done = sem("p_tot_done")
        z_ready = sem("z_ready")
        sg_ready = sem("sg_ready")
        y_ready = sem("y_ready")

        block = ctx.enter_context(nc.Block())

        def group(r, s):
            return RING * r + s

        def pair(r, s):
            return (RING // 2) * r + s // 2

        def squares_by(r, s, c):
            return CHUNKS * group(r, s) + c + 1

        def adds_by(r, s):
            return 1 + DVE_PER_PAIR * pair(r, s) + (CHUNKS if s % 2 == 0 else DVE_PER_PAIR)

        BODY = RING - END
        SQUARES = squares_by(ROUNDS - 1, BODY - 1, CHUNKS - 1)
        ADDS = adds_by(ROUNDS - 1, BODY - 1)
        PAIRS = pair(ROUNDS - 1, BODY - 1) + 1

        def unit(i, h):
            return h * END + i

        def adds_with(i, h):
            return ADDS + min(unit(i, h) + 1, 2 * END - 1)

        def half(h):
            return slice(h * HALF, (h + 1) * HALF)

        @block.sync
        def _(sp):
            sp.dma_start(xf[:, :], x_first).then_inc(first_landed, 16)
            for s in range(RING):
                sp.dma_start(xr[:, s].rearrange("p c b -> p (c b)"), x_groups[s]).then_inc(x_landed[s], 16)

            def free(r, s):
                sp.wait_ge(lin_used, group(r - 1, s) + 1)
                sp.wait_ge(squared, squares_by(r - 1, s, CHUNKS - 1))

            def load(r, s):
                free(r, s)
                sp.dma_start(xr[:, s].rearrange("p c b -> p (c b)"),
                             x_groups[bass.ds(group(r, s), 1)].rearrange("g p n -> (g p) n")
                             ).then_inc(x_landed[s], 16)

            with sp.Fori(1, ROUNDS - 1) as r:
                for s in range(RING):
                    load(r, s)
            for s in range(BODY):
                load(ROUNDS - 1, s)
            for h in range(2):
                for i in range(END):
                    if h == 0:
                        free(ROUNDS - 1, BODY + i)
                    x_chunks = x_groups[GROUPS - END + i].rearrange("p (c b) -> p c b", c=CHUNKS)
                    sp.dma_start(xr[:, BODY + i, :, half(h)], x_chunks[:, :, half(h)]).then_inc(end_landed[i][h], 16)
                sp.dma_start(xl[0:LAST, half(h)], x_last[:, half(h)]).then_inc(last_landed[h], 16)
            sp.wait_ge(y_ready, 1)
            sp.dma_start(out_rows, y[0:P:32, :].rearrange("t (h b) -> t h b", h=2)).then_inc(y_stored, 16)
            sp.wait_ge(y_stored, 16)

        @block.gpsimd
        def _(pool):
            def place(r, s):
                nc.gpsimd.tensor_copy(
                    wr[:, s].rearrange("p c k -> p (c k)"),
                    w[:, bass.ds(1 + CHUNKS * group(r, s), CHUNKS), :].rearrange("p c k -> p (c k)")
                ).then_inc(wr_ready, 1)

            pool.wait_ge(s_ready, 1)
            for s in range(RING):
                place(0, s)
            with pool.Fori(1, ROUNDS) as r:
                for s in range(RING):
                    pool.wait_ge(lin_used, group(r - 1, s) + 1)
                    if s % 2 == 1:
                        pool.wait_ge(sq_used, pair(r - 1, s) + 1)
                    pool.wait_ge(added, adds_by(r - 1, s))
                    place(r, s)

        @block.scalar
        def _(act):
            act.dma_start(w[:, :, :].rearrange("p c k -> p (c k)"), w_all).then_inc(w_landed, 16)
            act.dma_start(wl[0:LAST, :], w_last).then_inc(wl_landed, 16)
            act.dma_start(pr[:, :], params).then_inc(pr_landed, 16)
            act.wait_ge(zero_set, 1)
            nc.scalar.activation(warm[:, :], zero[:, 0:1], ACT.Sigmoid)
            act.wait_ge(first_landed, 16)
            nc.scalar.activation(sqf[:, :], xf[:, :], ACT.Square).then_inc(sqf_ready, 1)

            def square(r, s):
                act.wait_ge(x_landed[s], 16 * (r + 1))
                if type(r) is not int or group(r, s) >= SQ:
                    act.wait_ge(added, adds_by(r, s - SQ))
                    if s % 2 == 1:
                        act.wait_ge(sq_used, pair(r, s - SQ) + 1)
                for c in range(CHUNKS):
                    nc.scalar.activation(sq[:, s % SQ, c, :], xr[:, s, c, :], ACT.Square).then_inc(squared, 1)

            for s in range(RING):
                square(0, s)
            with act.Fori(1, ROUNDS - 1) as r:
                for s in range(RING):
                    square(r, s)
            for s in range(BODY):
                square(ROUNDS - 1, s)

            def square_half(i, h):
                s = BODY + i
                act.wait_ge(end_landed[i][h], 16)
                if h == 0:
                    act.wait_ge(added, adds_by(ROUNDS - 1, s - SQ))
                    act.wait_ge(sq_used, pair(ROUNDS - 1, s - SQ) + s % 2)
                nc.scalar.activation(sq[:, s % SQ, :, half(h)], xr[:, s, :, half(h)], ACT.Square).then_inc(squared, 1)

            def copy_lin(h):
                act.wait_ge(p_lin_done, h + 1)
                for u in range(2):
                    nc.scalar.copy(lin[:, h, u, :], p_lin[h][:, u * QUART:(u + 1) * QUART]).then_inc(lin_ready, 1)

            def layer1(h):
                act.wait_ge(p_h1_done, 2 * h + 1)
                nc.scalar.activation(h1[:, h, 0, :], p_h1[0][:, 0:QUART], ACT.Relu,
                                     bias=pr[:, C_B1:C_B1 + 1]).then_inc(h1a_ready, 1)

            def layer2(h):
                act.wait_ge(p_h2_done, 2 * h + 1)
                nc.scalar.activation(h2[0:H2, h, 0, :], p_h2[0:H2, 0:QUART], ACT.Relu,
                                     bias=pr[0:H2, C_B2:C_B2 + 1]).then_inc(h2a_ready, 1)

            for i in range(END):
                square_half(i, 0)
            copy_lin(0)
            act.wait_ge(pr_landed, 16)
            square_half(0, 1)
            layer1(0)
            square_half(1, 1)
            square_half(2, 1)
            act.wait_ge(pads_set, 1)
            layer2(0)
            square_half(3, 1)
            copy_lin(1)
            layer1(1)
            act.wait_ge(p_es_done, 1)
            nc.scalar.activation(gsq[:, :], p_es[:, 0:QUART], ACT.Square).then_inc(gsq_ready, 1)
            layer2(1)
            act.wait_ge(bias_ready, 1)
            act.wait_ge(z_ready, 1)
            nc.scalar.activation(sg[:, :], z[:, :], ACT.Sigmoid, bias=bias[:, :]).then_inc(sg_ready, 1)

        @block.vector
        def _(dve):
            nc.vector.memset(zero[:, :], 0.0).then_inc(zero_set, 1)
            nc.vector.memset(acc[:, :], 0.0).then_inc(acc_set, 1)
            nc.vector.memset(h2[:, :, :, :], 0.0).then_inc(pads_set, 1)
            nc.vector.memset(sqs[:, :, :], 0.0).then_inc(pads_set, 1)
            dve.wait_ge(w_landed, 16)
            nc.vector.scalar_tensor_tensor(fsq[:, :, :], w[:, :, 0:EMB], -0.5, w[:, :, 0:EMB],
                                           ALU.mult, ALU.mult).then_inc(fsq_ready, 1)
            dve.wait_ge(wl_landed, 16)
            nc.vector.scalar_tensor_tensor(fsql[0:LAST, :], wl[0:LAST, 0:EMB], -0.5, wl[0:LAST, 0:EMB],
                                           ALU.mult, ALU.mult).then_inc(fsq_ready, 1)
            dve.wait_ge(fsq_ready, 1)
            nc.vector.tensor_reduce(w[:, :, LIN:WC], fsq[:, :, :], AX.X, ALU.add).then_inc(s_ready, 1)
            dve.wait_ge(fsq_ready, 2)
            nc.vector.tensor_reduce(wl[0:LAST, LIN:WC], fsql[0:LAST, :], AX.X, ALU.add).then_inc(s_ready, 1)
            dve.wait_ge(pr_landed, 16)
            nc.vector.tensor_tensor(bias[:, :], pr[:, C_BLIN:C_BLIN + 1], pr[:, C_B3:C_B3 + 1],
                                    ALU.add).then_inc(bias_ready, 1)

            dve.wait_ge(acc_set, 1)
            dve.wait_ge(s_ready, 1)
            dve.wait_ge(sqf_ready, 1)
            nc.vector.scalar_tensor_tensor(acc[:, :], sqf[:, :], w[:, 0, LIN:WC], acc[:, :],
                                           ALU.mult, ALU.add).then_inc(added, 1)

            def add(r, s):
                dve.wait_ge(wr_ready, group(r, s) + 1)
                chunks = CHUNKS if s % 2 == 0 else CHUNKS - 1
                for c in range(chunks):
                    dve.wait_ge(squared, squares_by(r, s, c))
                    dve.wait_ge(added, adds_by(r, s) - chunks + c)
                    nc.vector.scalar_tensor_tensor(acc[:, :], sq[:, s % SQ, c, :], wr[:, s, c, LIN:WC],
                                                   acc[:, :], ALU.mult, ALU.add).then_inc(added, 1)

            for s in range(RING):
                add(0, s)
            with dve.Fori(1, ROUNDS - 1) as r:
                for s in range(RING):
                    add(r, s)
            for s in range(BODY):
                add(ROUNDS - 1, s)

            def add_half(i, h):
                if unit(i, h) == 2 * END - 1:
                    return
                s = BODY + i
                dve.wait_ge(wr_ready, GROUPS - END + i + 1)
                dve.wait_ge(squared, SQUARES + unit(i, h) + 1)
                dve.wait_ge(added, adds_with(i, h) - 1)
                nc.vector.scalar_tensor_tensor(acc[:, half(h)], sq[:, s % SQ, 0, half(h)], wr[:, s, 0, LIN:WC],
                                               acc[:, half(h)], ALU.mult, ALU.add).then_inc(added, 1)

            def product(h):
                dve.wait_ge(last_landed[h], 16)
                nc.vector.scalar_tensor_tensor(prod[0:LAST, half(h)], xl[0:LAST, half(h)], wl[0:LAST, LIN:WC],
                                               xl[0:LAST, half(h)], ALU.mult, ALU.mult).then_inc(prod_ready, 1)

            def layer1(h):
                dve.wait_ge(p_h1_done, 2 * h + 2)
                nc.vector.tensor_scalar(h1[:, h, 1, :], p_h1[1][:, 0:QUART], pr[:, C_B1:C_B1 + 1], 0.0,
                                        ALU.add, ALU.max).then_inc(h1b_ready, 1)

            def layer2(h):
                dve.wait_ge(p_h2_done, 2 * h + 2)
                nc.vector.tensor_scalar(h2[H2:P, h, 1, :], p_h2[H2:P, 0:QUART], pr[H2:P, C_B2:C_B2 + 1], 0.0,
                                        ALU.add, ALU.max).then_inc(h2b_ready, 1)

            add_half(0, 0)
            dve.wait_ge(pads_set, 2)
            dve.wait_ge(sq_used, PAIRS)
            for h in range(2):
                rows = slice(h * P // 2, (h + 1) * P // 2)
                nc.vector.tensor_copy(sqs[rows, h, :], p_sq[rows, :]).then_inc(sqs_ready, 1)
            for i in range(1, END):
                add_half(i, 0)
            dve.wait_ge(s_ready, 2)
            product(0)
            layer1(0)
            add_half(0, 1)
            add_half(1, 1)
            layer2(0)
            for i in range(2, END):
                add_half(i, 1)
            product(1)
            layer1(1)
            layer2(1)
            dve.wait_ge(gsq_ready, 1)
            dve.wait_ge(p_tot_done, 1)
            nc.vector.scalar_tensor_tensor(z[:, :], gsq[:, :], 0.5, p_tot[:, 0:QUART],
                                           ALU.mult, ALU.add).then_inc(z_ready, 1)
            dve.wait_ge(sg_ready, 1)
            nc.vector.tensor_scalar(y[:, :], sg[:, :], 5.0, 0.5, ALU.mult, ALU.add).then_inc(y_ready, 1)

        @block.tensor
        def _(pe):
            def add_mm(out, lhsT, rhs):
                return nc.tensor.matmul(out, lhsT, rhs, start=False, stop=False, skip_group_check=True)

            def tile_rows(ps, tile, rows, width=HALF):
                return ps[32 * tile:32 * tile + rows, 0:width]

            pe.wait_ge(zero_set, 1)
            for ps in (*p_lin, p_sq, p_tot, p_es):
                nc.tensor.matmul(ps[:, :], zero[:, 0:P], zero[:, :], start=True, stop=False, skip_group_check=True)

            pe.wait_ge(first_landed, 16)
            pe.wait_ge(w_landed, 16)
            for h in range(2):
                add_mm(tile_rows(p_lin[h], 2 * h, LIN), w[:, 0, 0:LIN], xf[:, half(h)])

            def squares_of_pair(r, s):
                pe.wait_ge(squared, squares_by(r, s, CHUNKS - 1))
                c, s = CHUNKS - 1, s % RING
                for h in range(2):
                    mm = add_mm(tile_rows(p_sq, 2 * h + s // 2 % 2, 1), wr[:, s, c, LIN:WC],
                                sq[:, s % SQ, c, half(h)])
                mm.then_inc(sq_used, 1)

            def multiply(r, s):
                pe.wait_ge(x_landed[s], 16 * (r + 1))
                pe.wait_ge(wr_ready, group(r, s) + 1)
                for c in range(CHUNKS):
                    for h in range(2):
                        mm = add_mm(tile_rows(p_lin[h], 2 * h + c, LIN), wr[:, s, c, 0:LIN], xr[:, s, c, half(h)])
                mm.then_inc(lin_used, 1)
                if s % 2 == 0 and not (type(r) is int and group(r, s) == 0):
                    squares_of_pair(r, s - 1)

            for s in range(RING):
                multiply(0, s)
            with pe.Fori(1, ROUNDS - 1) as r:
                for s in range(RING):
                    multiply(r, s)
            for s in range(BODY):
                multiply(ROUNDS - 1, s)

            def col(i):
                return pr[:, i:i + 1]

            def multiply_half(i, h):
                s = BODY + i
                pe.wait_ge(end_landed[i][h], 16)
                pe.wait_ge(wr_ready, GROUPS - END + i + 1)
                for c in range(CHUNKS):
                    for u in range(2):
                        t, q = 2 * c + u, slice(u * QUART, (u + 1) * QUART)
                        add_mm(p_lin[h][32 * t:32 * t + LIN, q], wr[:, s, c, 0:LIN],
                               xr[:, s, c, h * HALF + u * QUART:h * HALF + (u + 1) * QUART])

            def multiply_last(h):
                pe.wait_ge(last_landed[h], 16)
                for t in range(4):
                    mm = add_mm(p_lin[h][32 * t:32 * t + LIN, t * EIGHTH:(t + 1) * EIGHTH], wl[0:LAST, 0:LIN],
                                xl[0:LAST, h * HALF + t * EIGHTH:h * HALF + (t + 1) * EIGHTH])
                mm.then_inc(p_lin_done, 1)

            def rows(ps, h, lhsT, rhs):
                for t in range(4):
                    mm = add_mm(ps[32 * t:32 * t + 1, h * EIGHTH:(h + 1) * EIGHTH], lhsT(t), rhs(t))
                return mm

            def eighth(a, t):
                return a[:, t * EIGHTH:(t + 1) * EIGHTH]

            def lin_eighth(h, t):
                return eighth(lin[:, h].rearrange("p u b -> p (u b)"), t)

            def layer1(h):
                for u in range(2):
                    pe.wait_ge(lin_ready, 2 * h + u + 1)
                    if h == 1:
                        pe.wait_ge(h1a_ready if u == 0 else h1b_ready, 1)
                    nc.tensor.matmul(p_h1[u][:, 0:QUART], pr[:, C_W1:C_W1 + H1], lin[:, h, u, :],
                                     start=True, stop=True).then_inc(p_h1_done, 1)

            def layer2(h):
                for u in range(2):
                    if h == 1:
                        pe.wait_ge(h2a_ready if u == 0 else h2b_ready, 1)
                    pe.wait_ge(h1a_ready if u == 0 else h1b_ready, h + 1)
                    nc.tensor.matmul(p_h2[u * H2:(u + 1) * H2, 0:QUART], pr[:, C_W2:C_W2 + H2], h1[:, h, u, :],
                                     start=True, stop=True).then_inc(p_h2_done, 1)

            def layer3(h):
                pe.wait_ge(h2a_ready, h + 1)
                pe.wait_ge(h2b_ready, h + 1)
                return rows(p_tot, h, lambda t: col(C_W3 + t // 2),
                            lambda t: h2[:, h, t // 2, t % 2 * EIGHTH:(t % 2 + 1) * EIGHTH])

            def embedding_sum(h):
                return rows(p_es, h, lambda t: col(C_SE), lambda t: lin_eighth(h, t))

            def linear_term(h):
                rows(p_tot, h, lambda t: col(C_SX), lambda t: lin_eighth(h, t))

            def own_squares(h):
                rows(p_tot, h, lambda t: col(C_ONE), lambda t: eighth(sqs[:, h], t))

            def added_squares(h):
                pe.wait_ge(added, adds_with(END - 1, h))
                rows(p_tot, h, lambda t: col(C_ONE), lambda t: eighth(acc[:, half(h)], t))

            def last_squares(h):
                pe.wait_ge(prod_ready, h + 1)
                rows(p_tot, h, lambda t: pr[0:LAST, C_ONE:C_ONE + 1], lambda t: eighth(prod[0:LAST, half(h)], t))

            def squares_of_half(i, h, c):
                pe.wait_ge(squared, SQUARES + unit(i, h) + 1)
                s = BODY + i
                rows(p_tot, h, lambda t: wr[:, s, c, LIN:WC], lambda t: eighth(sq[:, s % SQ, c, half(h)], t))

            multiply_half(0, 0)
            squares_of_pair(ROUNDS - 1, BODY - 1)
            for i in range(1, END):
                multiply_half(i, 0)
                squares_of_half(i - 1, 0, 1)
            pe.wait_ge(pr_landed, 16)
            pe.wait_ge(sqs_ready, 2)
            own_squares(0)
            own_squares(1)
            pe.wait_ge(wl_landed, 16)
            multiply_last(0)
            squares_of_half(END - 1, 0, 1)

            multiply_half(0, 1)
            layer1(0)
            embedding_sum(0)
            linear_term(0)
            multiply_half(1, 1)
            squares_of_half(0, 1, 1)
            added_squares(0)
            last_squares(0)
            layer2(0)
            multiply_half(2, 1)
            squares_of_half(1, 1, 1)
            layer3(0)
            multiply_half(3, 1)
            multiply_last(1)
            squares_of_half(2, 1, 1)
            added_squares(1)

            layer1(1)
            embedding_sum(1).then_inc(p_es_done, 1)
            linear_term(1)
            layer2(1)
            squares_of_half(3, 1, 0)
            squares_of_half(3, 1, 1)
            last_squares(1)
            layer3(1).then_inc(p_tot_done, 1)


def kernel(r_input_data, L0_rec_W_lin, L0_rec_b_lin, L0_rec_factors, L0_rec_W1, L0_rec_b1, L0_rec_W2, L0_rec_b2,
           L0_rec_W3, L0_rec_b3):
    import numpy as np
    import concourse.bacc as bacc
    from concourse.bass_utils import run_bass_kernel_spmd

    f32 = np.float32
    xT = np.ascontiguousarray(np.asarray(r_input_data).T)
    wrow = np.concatenate([np.asarray(L0_rec_factors), np.asarray(L0_rec_W_lin).T, np.zeros((N, 1), f32)], axis=1)
    w_groups = wrow[P:N - LAST].reshape(GROUPS, P, CHUNKS * WC).transpose(1, 0, 2).reshape(P, -1)
    w_all = np.ascontiguousarray(np.concatenate([wrow[:P], w_groups], axis=1))
    w_last = np.ascontiguousarray(wrow[N - LAST:])

    params = np.zeros((P, C_ALL), f32)
    for t in range(4):
        params[32 * t:32 * t + EMB, C_W1:C_W1 + H1] = np.asarray(L0_rec_W1).T
        params[32 * t:32 * t + EMB, C_SE] = 1.0
        params[32 * t + EMB, C_SX] = 1.0
    params[:, C_W2:C_W2 + H2] = np.asarray(L0_rec_W2).T
    params[:, C_B1] = np.asarray(L0_rec_b1)
    for h in range(2):
        params[h * H2:(h + 1) * H2, C_B2] = np.asarray(L0_rec_b2)
        params[h * H2:(h + 1) * H2, C_W3 + h] = np.asarray(L0_rec_W3)[0]
    params[:, C_BLIN] = np.asarray(L0_rec_b_lin)
    params[:, C_B3] = np.asarray(L0_rec_b3)
    params[:, C_ONE] = 1.0

    arrays = {"xT": xT, "w_all": w_all, "w_last": w_last, "params": params}
    nc = bacc.Bacc("TRN2", target_bir_lowering=False, num_devices=1)
    args = [nc.dram_tensor(f"in_{name}", a.shape, F32, kind="ExternalInput").ap() for name, a in arrays.items()]
    out = nc.dram_tensor("out_y", (B,), F32, kind="ExternalOutput").ap()
    fm_kernel(nc, *args, out)
    r = run_bass_kernel_spmd(nc, [{f"in_{name}": a for name, a in arrays.items()}], core_ids=[0])
    return r.results[0]["out_y"]
```
